# Optimizing a Trainium2 kernel written in Bass

```python
import numpy as np
import jax
import jax.numpy as jnp

def _softmax(x, axis=-1):
    return jax.nn.softmax(x, axis=axis)

def _gelu(x):
    return jax.nn.gelu(x, approximate=True)

def _silu(x):
    return jax.nn.silu(x)

def _sigmoid(x):
    return jax.nn.sigmoid(x)

def _layernorm(x, axis=-1, eps=1e-05):
    m = jnp.mean(x, axis=axis, keepdims=True)
    v = jnp.var(x, axis=axis, keepdims=True)
    return (x - m) / jnp.sqrt(v + eps)

def _scatter_add(tgt, idx, src, axis=0):
    return tgt.at[idx].add(src)

def _segment_sum(src, seg, n):
    return jax.ops.segment_sum(src, seg, n)
kernel_name = 'mk_gnn_ffn_d1_gnn_r8_fdb212'

def setup_inputs(seed: int=0):
    np.random.seed(seed)
    _w = jnp.asarray

    def _rec_inputs():
        import jax
        import jax.numpy as jnp
        _gk = jax.random.key(seed)
        x = -0.0002117 + 1 * jax.random.normal(jax.random.fold_in(_gk, 1), (3125, 1024), jnp.float32)
        src = jax.random.randint(jax.random.fold_in(_gk, 2), (50000,), 0, 3125, jnp.int32)
        dst = jnp.minimum((3125 * jax.random.uniform(jax.random.fold_in(_gk, 3), (50000,)) ** 2.0).astype(jnp.int32), 24999)
        _o = jnp.argsort(dst, stable=True)
        src = src[_o]
        dst = dst[_o]
        return (x, src, dst)
    x, src, dst = _rec_inputs()

    def _L0_gnn_setup():
        import jax, jax.numpy as jnp
        import numpy as np
        N = 3125
        E = 50000
        H = 4
        C = 256
        D_IN = 1024
        NEG_SLOPE = 0.2
        key = jax.random.key(seed)
        k1, k2, k3, k4, k5, k6 = jax.random.split(key, 6)
        x = jax.random.normal(k1, (N, D_IN), dtype=jnp.float32)
        edge_index = jax.random.randint(k2, (2, E), 0, N, dtype=jnp.int64)
        scale = 1.0 / np.sqrt(D_IN)
        W = jax.random.normal(k3, (D_IN, H * C), dtype=jnp.float32) * scale
        att_src = jax.random.normal(k4, (H, C), dtype=jnp.float32) * 0.1
        att_dst = jax.random.normal(k5, (H, C), dtype=jnp.float32) * 0.1
        bias = jax.random.normal(k6, (H * C,), dtype=jnp.float32) * 0.01
        return {'x': x, 'edge_index': edge_index, 'W': W, 'att_src': att_src, 'att_dst': att_dst, 'bias': bias}
    _L0_gnn_all = _L0_gnn_setup()
    _L0_gnn_in = {k: v for k, v in _L0_gnn_all.items() if k in ('W', 'att_src', 'att_dst', 'bias')}
    del _L0_gnn_all

    def _L0_ffn_setup():
        import jax, jax.numpy as jnp
        import numpy as np
        ALPHA = 1.702
        LIMIT = 9.0
        TOP_K = 2

        def swiglu(x):
            g, v = (x[..., 0::2], x[..., 1::2])
            g = jnp.clip(g, None, LIMIT)
            v = jnp.clip(v, -LIMIT, LIMIT)
            return g * jax.nn.sigmoid(ALPHA * g) * (v + 1)
        key = jax.random.key(seed)
        ks = jax.random.split(key, 6)
        B, L, D = (2, 256, 1024)
        E, F = (8, 256)
        s_gate = 1.0 / np.sqrt(D)
        s1 = 1.0 / np.sqrt(D)
        s2 = 1.0 / np.sqrt(F)
        return {'x': jax.random.normal(ks[0], (B, L, D), dtype=jnp.float32), 'gate_w': jax.random.normal(ks[1], (D, E), dtype=jnp.float32) * s_gate, 'dense_1_w': jax.random.normal(ks[2], (E, 2 * F, D), dtype=jnp.float32) * s1, 'dense_1_b': jnp.zeros((E, 2 * F), dtype=jnp.float32), 'dense_2_w': jax.random.normal(ks[3], (E, D, F), dtype=jnp.float32) * s2, 'dense_2_b': jnp.zeros((E, D), dtype=jnp.float32)}
    _L0_ffn_all = _L0_ffn_setup()
    _L0_ffn_in = {k: v for k, v in _L0_ffn_all.items() if k in ('gate_w', 'dense_1_w', 'dense_1_b', 'dense_2_w', 'dense_2_b')}
    del _L0_ffn_all
    return {'x': x, 'src': src, 'dst': dst, 'L0_gnn_W': _L0_gnn_in['W'], 'L0_gnn_att_src': _L0_gnn_in['att_src'], 'L0_gnn_att_dst': _L0_gnn_in['att_dst'], 'L0_gnn_bias': _L0_gnn_in['bias'], 'L0_ffn_gate_w': _L0_ffn_in['gate_w'], 'L0_ffn_dense_1_w': _L0_ffn_in['dense_1_w'], 'L0_ffn_dense_1_b': _L0_ffn_in['dense_1_b'], 'L0_ffn_dense_2_w': _L0_ffn_in['dense_2_w'], 'L0_ffn_dense_2_b': _L0_ffn_in['dense_2_b']}

def reference(x, src, dst, L0_gnn_W, L0_gnn_att_src, L0_gnn_att_dst, L0_gnn_bias, L0_ffn_gate_w, L0_ffn_dense_1_w, L0_ffn_dense_1_b, L0_ffn_dense_2_w, L0_ffn_dense_2_b):
    import jax
    import jax.numpy as jnp

    def _L0_gnn_ref(x, edge_index, W, att_src, att_dst, bias):
        import jax, jax.numpy as jnp
        import numpy as np
        N = 3125
        E = 50000
        H = 4
        C = 256
        D_IN = 1024
        NEG_SLOPE = 0.2
        xp = (x @ W).reshape(N, H, C)
        a_src = jnp.einsum('nhc,hc->nh', xp, att_src)
        a_dst = jnp.einsum('nhc,hc->nh', xp, att_dst)
        loops = jnp.arange(N, dtype=edge_index.dtype)
        src = jnp.concatenate([edge_index[0], loops])
        dst = jnp.concatenate([edge_index[1], loops])
        e = jax.nn.leaky_relu(a_src[src] + a_dst[dst], NEG_SLOPE)
        m = jax.ops.segment_max(e, dst, num_segments=N)
        ee = jnp.exp(e - m[dst])
        z = jax.ops.segment_sum(ee, dst, num_segments=N)
        alpha = ee / z[dst]
        msgs = xp[src] * alpha[:, :, None]
        out = jax.ops.segment_sum(msgs, dst, num_segments=N)
        out = out.reshape(N, H * C) + bias
        return jax.nn.relu(out)

    def _L0_ffn_ref(x, gate_w, dense_1_w, dense_1_b, dense_2_w, dense_2_b):
        import jax, jax.numpy as jnp
        import numpy as np
        ALPHA = 1.702
        LIMIT = 9.0
        TOP_K = 2

        def swiglu(x):
            g, v = (x[..., 0::2], x[..., 1::2])
            g = jnp.clip(g, None, LIMIT)
            v = jnp.clip(v, -LIMIT, LIMIT)
            return g * jax.nn.sigmoid(ALPHA * g) * (v + 1)
        B, L, D = x.shape
        xf = x.reshape(B * L, D)
        gate = xf @ gate_w
        weights, sel = jax.lax.top_k(gate, k=TOP_K)
        weights = jax.nn.softmax(weights, axis=-1)
        h = jnp.einsum('ecd,td->tec', dense_1_w, xf) + dense_1_b[None]
        h = swiglu(h)
        y = jnp.einsum('edf,tef->ted', dense_2_w, h) + dense_2_b[None]
        y_sel = jnp.take_along_axis(y, sel[:, :, None], axis=1)
        out = jnp.einsum('tkd,tk->td', y_sel, weights)
        return out.reshape(B, L, D)
    edge_index = jnp.stack([src, dst])
    x = x + _L0_gnn_ref(_layernorm(x, axis=-1), edge_index, L0_gnn_W, L0_gnn_att_src, L0_gnn_att_dst, L0_gnn_bias)
    x = x + _L0_ffn_ref(_layernorm(x, axis=-1)[None], L0_ffn_gate_w, L0_ffn_dense_1_w, L0_ffn_dense_1_b, L0_ffn_dense_2_w, L0_ffn_dense_2_b)[0]
    return x

_drawn_inputs = setup_inputs


def setup_inputs(seed=0):
    import zlib

    import numpy as np

    out = dict(_drawn_inputs(seed))
    spreads = {'L0_ffn_dense_1_b': (0.0, 0.1), 'L0_ffn_dense_2_b': (0.0, 0.1)}
    factors = {}
    for name, (base, spread) in spreads.items():
        noise = np.random.default_rng([zlib.crc32(name.encode()), seed]).standard_normal(out[name].shape)
        drawn = base * np.exp(spread * noise) if base else spread * noise
        out[name] = jnp.asarray(drawn.astype(out[name].dtype))
    for name, factor in factors.items():
        out[name] = (out[name] * factor).astype(out[name].dtype)
    return out
```

```python
from contextlib import ExitStack

import concourse.bass as bass
from concourse import mybir

F32 = mybir.dt.float32
I32 = mybir.dt.int32
BF16 = mybir.dt.bfloat16
ALU = mybir.AluOpType
ACT = mybir.ActivationFunctionType
AX = mybir.AxisListType

P = 128
BIG = 1e30
EPS = 1e-5
NEG_SLOPE = 0.2
ALPHA = 1.702
LIMIT = 9.0


def gat_moe_kernel(nc, x, src, dst, w, w_t, att_src, att_dst, bias, gate_t, w1, b1, w2, b2, out):
    N, D = x.shape
    E = src.shape[0]
    H, C = att_src.shape
    NE, _, _, F2 = w1.shape
    F = F2 // 2
    KT = D // P
    FT = F // P
    NT = -(-N // P)
    LAST = N - (NT - 1) * P
    ET = -(-E // (4 * P)) * 4
    RQ = ET // 4
    CH = 16
    PAIRS = -(-(-(-E // P) + NT - 1) // CH) * CH
    PQ = PAIRS // 4
    NCH = PAIRS // CH
    CE = CH * P
    SLOTS = (2 * N + NE * (P - 1)) // P
    NCOL = 2 * H + 1
    assert H * C == D and NCH == NT + 1 and NT % 2 == 1 and SLOTS % 8 == 0 and PAIRS // P < ET

    def dram(name, shape, dt):
        return nc.dram_tensor(name, shape, dt, kind="Internal").ap()

    src_tiles = dram("src_tiles", [ET, P], I32)
    dst_tiles = dram("dst_tiles", [ET, P], I32)
    lows = dram("lows", [2, PAIRS * P], BF16)
    tile_list = dram("tile_list", [PAIRS], I32)
    xln_t = dram("xln_t", [NT, P, D], F32)
    xp = dram("xp", [NT * P, D], F32)
    x1_d = dram("x1_d", [NT * P, D], F32)
    x2_d = dram("x2_d", [NT * P, D], F32)
    y_d = dram("y_d", [SLOTS * P, D], F32)

    ctx = ExitStack()
    with ctx:
        def sem(name):
            return ctx.enter_context(nc.semaphore(name))

        def place(stack, name, shape, dt=F32):
            return stack.enter_context(nc.sbuf_tensor(name, shape, dt))

        ps = ctx.enter_context(nc.psum_tensor("ps", [P, 8, 512], F32))

        ident = place(ctx, "ident", [P, P])
        iota = place(ctx, "iota", [P, P])
        lane = place(ctx, "lane", [P, 1])
        upper = place(ctx, "upper", [P, P])
        ones = place(ctx, "ones", [P, P])
        zero_col = place(ctx, "zero_col", [P, 1])
        eps_col = place(ctx, "eps_col", [P, 1])
        tile_row = place(ctx, "tile_row", [1, PAIRS + 1], I32)
        start_row = place(ctx, "start_row", [1, NT + 1], I32)
        pair_cols = place(ctx, "pair_cols", [P, PAIRS, NCOL])
        pair_dst = place(ctx, "pair_dst", [P, PAIRS])
        pair_src = place(ctx, "pair_src", [P, PAIRS], I32)
        gate_all = place(ctx, "gate_all", [P, NT, NE])

        XS = 4
        part1 = ExitStack()
        part1a = ExitStack()
        wt_sb = place(part1a, "wt_sb", [P, KT, D])
        x_in = place(part1a, "x_in", [P, XS, D])
        xln = place(part1a, "xln", [P, 2, D])
        xt_out = place(part1a, "xt_out", [P, XS, KT, P])
        left = nc.sbuf_bytes_remaining
        part1a.close()
        xt_in = place(part1, "xt_in", [P, 2, KT, P])
        xp_out = place(part1, "xp_out", [P, 2, D])
        part1c = ExitStack()
        as_rows = place(part1c, "as_rows", [PQ, H, 4 * P])
        fwd = place(part1c, "fwd", [PQ, H, 4 * P])
        bwd = place(part1c, "bwd", [PQ, H, 4 * P])
        max_col = place(part1c, "max_col", [P, PAIRS, H])
        z_col = place(part1c, "z_col", [P, 3, PAIRS, H])
        left = min(left, nc.sbuf_bytes_remaining)
        part1c.close()
        lows_in = place(part1, "lows_in", [P, 2, 2, CE], BF16)
        lows_hot = place(part1, "lows_hot", [P, 2, 2, CE], BF16)
        picked = place(part1, "picked", [P, 2, 4, NT, H])
        hi_hot = place(part1, "hi_hot", [P, PAIRS, NT], BF16)

        if nc.sbuf_bytes_remaining > left:
            place(part1, "spare", [P, (nc.sbuf_bytes_remaining - left) // 4])

        w_sb = place(part1, "w_sb", [P, KT, D])
        att_in = place(part1, "att_in", [P, 2, KT])
        att_blk = place(part1, "att_blk", [P, KT, 2 * H])
        w_att = place(part1, "w_att", [P, KT, 2 * H])
        stats = place(part1, "stats", [P, XS, 2, 6])
        mv = place(part1, "mv", [P, XS, 2])
        std = place(part1, "std", [P, XS, 1])
        rstd = place(part1, "rstd", [P, XS, 1])
        rows_in = place(part1, "rows_in", [RQ, 2, 4 * P], I32)
        dst_f = place(part1, "dst_f", [RQ, 4 * P])
        below = place(part1, "below", [RQ, 4 * P])
        node_att = place(part1, "node_att", [P, NT, 2 * H])
        node_res = place(part1, "node_res", [P, 2, NT, 2 * H])
        node_parts = place(part1, "node_parts", [P, 3, NT, 2 * H], BF16)
        as_col = place(part1, "as_col", [P, PAIRS, H])
        dst_col = place(part1, "dst_col", [P, PAIRS, 2 * H])
        hi_col = place(part1, "hi_col", [P, PAIRS])
        last_col = place(part1, "last_col", [P, PAIRS])
        count_part = place(part1, "count_part", [RQ, NT - 1])
        count_i = place(part1, "count_i", [P, 2, NT - 1], I32)
        start_f = place(part1, "start_f", [P, NT - 1])
        start_all = place(part1, "start_all", [1, NT + 1])
        reached = place(part1, "reached", [PQ, NT - 1])
        pair_id = place(part1, "pair_id", [PQ, 4])
        tile_f = place(part1, "tile_f", [PQ, 4])
        tile_i = place(part1, "tile_i", [PQ, 4], I32)
        etile_i = place(part1, "etile_i", [PQ, 4], I32)
        minus_base = place(part1, "minus_base", [PQ, 4])
        pair_rows = place(part1, "pair_rows", [PQ, 2, 4 * P], I32)
        int_rows = place(part1, "int_rows", [PQ, 2, 4 * P], I32)
        low_rows = place(part1, "low_rows", [PQ, 2, 4 * P], BF16)
        hi_rows = place(part1, "hi_rows", [PQ, 4 * P])
        src_rows = place(part1, "src_rows", [PQ, 4 * P])
        dst_rows = place(part1, "dst_rows", [PQ, 4 * P])
        rel_rows = place(part1, "rel_rows", [PQ, 4 * P])
        valid = place(part1, "valid", [PQ, 4 * P])
        key = place(part1, "key", [PQ, 4 * P])
        differs = place(part1, "differs", [PQ, 4 * P + 1])
        reset = place(part1, "reset", [PQ, 4 * P + 1])
        last_rows = place(part1, "last_rows", [PQ, 4 * P])
        ends = place(part1, "ends", [PQ, 4, H])
        ends_t = place(part1, "ends_t", [H, 4, PQ])
        joins = place(part1, "joins", [H, PQ + 1])
        whole = place(part1, "whole", [H, PQ])
        chain = place(part1, "chain", [H, 2, PQ])
        scan_t = place(part1, "scan_t", [H, 2, PQ])
        carry_t = place(part1, "carry_t", [H, 3, PQ])
        carry = place(part1, "carry", [PQ, 3, H])
        part1.close()

        GR = 8
        part2 = ExitStack()
        dst_hot = place(part2, "dst_hot", [P, 2 * CH, P])
        weighted = place(part2, "weighted", [P, GR, H, P])
        messages = place(part2, "messages", [P, GR, D])
        message_idx = place(part2, "message_idx", [P, CH], I32)
        gate_b = place(part2, "gate_b", [P, NE, D])
        bias_b = place(part2, "bias_b", [P, D])
        x_own = place(part2, "x_own", [P, 2 * D])
        xp_own = place(part2, "xp_own", [P, 2 * D])
        summed = place(part2, "summed", [P, D])
        x1_sb = place(part2, "x1_sb", [P, D])
        x2_sb = place(part2, "x2_sb", [P, D])
        gate_now = place(part2, "gate_now", [P, NE])
        product = place(part2, "product", [P, D])
        sums = place(part2, "sums", [P, NCOL])
        no_edge = place(part2, "no_edge", [P, 1])
        own_w = place(part2, "own_w", [P, H])
        total = place(part2, "total", [P, H])
        inv_total = place(part2, "inv_total", [P, H])
        own_share = place(part2, "own_share", [P, H])
        stats2 = place(part2, "stats2", [P, 2, 6])
        mv2 = place(part2, "mv2", [P, 2])
        var2 = place(part2, "var2", [P, 1])
        half2 = place(part2, "half2", [P, 1])
        guess_i = place(part2, "guess_i", [P, 1], I32)
        root2 = place(part2, "root2", [P, 1])
        square2 = place(part2, "square2", [P, 1])
        part2.close()

        part3 = ExitStack()
        part3a = ExitStack()
        y_first = place(part3a, "y_first", [P, 2, D])
        y_second = place(part3a, "y_second", [P, 2, D])
        x1_in = place(part3a, "x1_in", [P, 2, D])
        partial = place(part3a, "partial", [P, D])
        out_sb = place(part3a, "out_sb", [P, 2, D])
        left = nc.sbuf_bytes_remaining
        part3a.close()
        w1_sb = place(part3, "w1_sb", [P, 2, KT, F2])
        w2_sb = place(part3, "w2_sb", [P, 2, FT, D])
        assert nc.sbuf_bytes_remaining <= left
        b1_b = place(part3, "b1_b", [P, NE, F2])
        b2_b = place(part3, "b2_b", [P, NE, D])
        token_idx = place(part3, "token_idx", [P, SLOTS], I32)
        idx_ring = place(part3, "idx_ring", [P, 8], I32)
        slots_i = place(part3, "slots_i", [P, NT, 2], I32)
        mix = place(part3, "mix", [P, NT, 2])
        expert_row = place(part3, "expert_row", [1, SLOTS], I32)
        expert_end = place(part3, "expert_end", [1, NE], I32)
        part3b = ExitStack()
        lane_hot = place(part3b, "lane_hot", [P, NT * 2, P])
        tile_hot = place(part3b, "tile_hot", [P, NT * 2, SLOTS])
        best = place(part3b, "best", [P, 2, NT])
        is_best = place(part3b, "is_best", [P, NT, NE])
        rank = place(part3b, "rank", [P, NT, NE])
        rank_best = place(part3b, "rank_best", [P, NT])
        chosen = place(part3b, "chosen", [P, 2, NT, NE])
        gate_rest = place(part3b, "gate_rest", [P, NT, NE])
        selected = place(part3b, "selected", [P, NT, NE])
        real_node = place(part3b, "real_node", [P, 1])
        far = place(part3b, "far", [P, 1])
        reversed_e = place(part3b, "reversed_e", [P, NE])
        per_tile = place(part3b, "per_tile", [P, NE, NT])
        goes_on = place(part3b, "goes_on", [P, NE, NT])
        so_far = place(part3b, "so_far", [P, NE, NT])
        count_e = place(part3b, "count_e", [P, NE])
        tiles_ei = place(part3b, "tiles_ei", [P, 2, NE], I32)
        tiles_e = place(part3b, "tiles_e", [P, NE])
        ends_e = place(part3b, "ends_e", [P, NE])
        first_slot = place(part3b, "first_slot", [P, NE])
        position = place(part3b, "position", [P, NT, NE])
        slot_f = place(part3b, "slot_f", [P, NT, 2])
        slot_i = place(part3b, "slot_i", [P, NT, 2], I32)
        slot_lane_i = place(part3b, "slot_lane_i", [P, NT * 2], I32)
        slot_tile_i = place(part3b, "slot_tile_i", [P, NT * 2], I32)
        slot_lane = place(part3b, "slot_lane", [P, NT * 2])
        slot_tile = place(part3b, "slot_tile", [P, NT * 2])
        token_id = place(part3b, "token_id", [P, NT, 2])
        gap = place(part3b, "gap", [P, NT])
        e_gap = place(part3b, "e_gap", [P, NT])
        at_end = place(part3b, "at_end", [1, SLOTS, NE])
        expert_f = place(part3b, "expert_f", [1, SLOTS])
        part3b.close()
        tokens_in = place(part3, "tokens_in", [P, 4, D])
        tokens_t = place(part3, "tokens_t", [P, 2, KT, P])
        h_sb = place(part3, "h_sb", [P, 2, F2])
        g_sb = place(part3, "g_sb", [P, 2, F])
        sig_sb = place(part3, "sig_sb", [P, 2, F])
        v_sb = place(part3, "v_sb", [P, 2, F])
        gv_sb = place(part3, "gv_sb", [P, 2, F])
        act_sb = place(part3, "act_sb", [P, 2, F])
        act_t = place(part3, "act_t", [P, 2, FT, P])
        y_sb = place(part3, "y_sb", [P, 2, D])
        part3.close()

        consts = sem("consts")
        cleared = sem("cleared")
        rows_loaded = sem("rows_loaded")
        tiles_stored = sem("tiles_stored")
        counted = sem("counted")
        counts_summed = sem("counts_summed")
        etiles_ready = sem("etiles_ready")
        pairs_gathered = sem("pairs_gathered")
        tile_list_stored = sem("tile_list_stored")
        tile_row_loaded = sem("tile_row_loaded")
        att_loaded = sem("att_loaded")
        att_placed = sem("att_placed")
        wt_loaded = sem("wt_loaded")
        w_att_summed = sem("w_att_summed")
        w_att_ready = sem("w_att_ready")
        w_loaded = sem("w_loaded")
        x_loaded = [sem(f"x_loaded{j}") for j in range(XS)]
        x_tail = sem("x_tail")
        stats_ready = sem("stats_ready")
        std_ready = sem("std_ready")
        xln_ready = sem("xln_ready")
        turned = sem("turned")
        xt_evacuated = sem("xt_evacuated")
        xt_stored = [sem(f"xt_stored{j}") for j in range(XS)]
        att_done = sem("att_done")
        parts_ready = sem("parts_ready")
        dve = sem("dve")
        lows_ready = sem("lows_ready")
        lows_stored = sem("lows_stored")
        rows_ready = sem("rows_ready")
        rows_turned = sem("rows_turned")
        cols_taken = sem("cols_taken")
        xt_loaded = [sem(f"xt_loaded{j}") for j in range(2)]
        projected = sem("projected")
        xp_evacuated = sem("xp_evacuated")
        xp_stored = [sem(f"xp_stored{j}") for j in range(2)]
        lows_loaded = [sem(f"lows_loaded{j}") for j in range(2)]
        hot_ready = sem("hot_ready")
        src_fetched = sem("src_fetched")
        src_taken = sem("src_taken")
        dst_fetched = sem("dst_fetched")
        dst_taken = sem("dst_taken")
        as_ready = sem("as_ready")
        as_turned = sem("as_turned")
        as_rows_ready = sem("as_rows_ready")
        ends_ready = sem("ends_ready")
        ends_turned = sem("ends_turned")
        carry_ready = sem("carry_ready")
        carry_turned = sem("carry_turned")
        max_ready = sem("max_ready")
        max_turned = sem("max_turned")
        max_taken = sem("max_taken")
        z_ready = sem("z_ready")
        exp_ready = sem("exp_ready")
        weights_ready = sem("weights_ready")
        xp_complete = sem("xp_complete")

        pair_done = sem("pair_done")
        hot_built = sem("hot_built")
        weighted_ready = sem("weighted_ready")
        message_loaded = [sem(f"message_loaded{j}") for j in range(GR)]
        idx_copied = sem("idx_copied")
        acc_free = sem("acc_free")
        own_loaded = sem("own_loaded")
        own_tail = sem("own_tail")
        epi = sem("epi")
        sums_loaded = sem("sums_loaded")
        x12_ready = sem("x12_ready")
        x12_stored = sem("x12_stored")
        phase2_done = sem("phase2_done")

        pool_turn = sem("pool_turn")
        sp_turn = sem("sp_turn")

        dve3 = sem("dve3")
        biases_loaded = sem("biases_loaded")
        expert_loaded = [sem(f"expert_loaded{j}") for j in range(2)]
        expert_seen = sem("expert_seen")
        gaps_ready = sem("gaps_ready")
        gap_exp = sem("gap_exp")
        selected_ready = sem("selected_ready")
        ranks_summed = sem("ranks_summed")
        lists_ready = sem("lists_ready")
        lane_hot_ready = sem("lane_hot_ready")
        ids_summed = sem("ids_summed")
        ids_ready = sem("ids_ready")
        rows_known = sem("rows_known")
        idx3 = sem("idx3")
        tokens_loaded = [sem(f"tokens_loaded{j}") for j in range(4)]
        tokens_turned = sem("tokens_turned")
        tokens_ready = sem("tokens_ready")
        h_ready = sem("h_ready")
        h_taken = sem("h_taken")
        g_ready = sem("g_ready")
        sig_ready = sem("sig_ready")
        act_ready = sem("act_ready")
        act_turned = sem("act_turned")
        act_t_ready = sem("act_t_ready")
        y_ready = sem("y_ready")
        y_taken = sem("y_taken")
        y_stored = [sem(f"y_stored{j}") for j in range(2)]
        y_complete = sem("y_complete")
        first_loaded = [sem(f"first_loaded{j}") for j in range(2)]
        x1_loaded = [sem(f"x1_loaded{j}") for j in range(2)]
        mixed = sem("mixed")
        out_stored = [sem(f"out_stored{j}") for j in range(2)]

        class Steps:

            def __init__(self, eng, s):
                self.eng, self.s, self.base, self.n = eng, s, 0, 0

            def mark(self, instruction):
                instruction.then_inc(self.s, 1)
                self.n += 1

            def wait(self):
                self.eng.wait_ge(self.s, self.base + self.n)

            def then(self, instruction):
                self.mark(instruction)
                self.wait()

            def rounds(self, i, per_round):
                self.first = self.base + self.n
                self.base, self.n, self.per = i * per_round + self.first, 0, per_round

            def end_rounds(self, count):
                assert self.n == self.per, (self.n, self.per)
                self.base, self.n = self.first + count * self.per, 0

        def tile_of(ap, t):
            return ap[bass.ds(t * P, P), :]

        block = ctx.enter_context(nc.Block())
        HALF = (NT - 1) // XS
        STEPS2 = (NT - 1) // 2 // 2

        @block.sync
        def _(sp):
            for s, depth in ((xln_ready, XS), (turned, 2), (xt_evacuated, 2), (att_done, XS),
                             (projected, 2), (xp_evacuated, 2), (src_taken, 2), (dst_fetched, 2),
                             (dst_taken, 2), *((q, 16) for q in xt_stored + xp_stored)):
                sp.sem_inc(s, depth)
            sp.wait_ge(cleared, 2)
            full = E // (4 * P)
            even = full // 16 * 16
            for n, edges in enumerate((src, dst)):
                sp.dma_start(rows_in[0:even, n, :],
                             edges[0:even * 4 * P].rearrange("(q f) -> q f", f=4 * P)).then_inc(rows_loaded, 16)
                sp.dma_start(rows_in[even:full, n, :],
                             edges[even * 4 * P:full * 4 * P].rearrange("(q f) -> q f", f=4 * P)).then_inc(rows_loaded, 16)
                sp.dma_start(rows_in[full:full + 1, n, 0:E - full * 4 * P],
                             edges[full * 4 * P:E].rearrange("(q f) -> q f", q=1)).then_inc(rows_loaded, 16)
            for n, att in enumerate((att_src, att_dst)):
                sp.dma_start(att_in[:, n, :], att.rearrange("h (a p) -> p (h a)", p=P),
                             allow_slow_non_contiguous=True).then_inc(att_loaded, 16)

            def load_x(t, j, k):
                sp.wait_ge(xln_ready, t + 1)
                sp.dma_start(x_in[:, j, :], tile_of(x, t)).then_inc(x_loaded[j], 16)

            for t in range(XS):
                load_x(t, t, 0)
                if t == 0:
                    sp.dma_start(wt_sb[:, :, :], w_t).then_inc(wt_loaded, 16)
            sp.wait_ge(rows_loaded, 96)
            for n, tiles in enumerate((src_tiles, dst_tiles)):
                sp.dma_start(tiles.rearrange("(q b) f -> q (b f)", b=4), rows_in[:, n, :]).then_inc(tiles_stored, 16)
            with sp.Fori(1, HALF) as i:
                for j in range(XS):
                    load_x(i * XS + j, j, i)
            sp.wait_ge(xln_ready, NT)
            t = NT - 1
            even = LAST // 16 * 16
            sp.dma_start(x_in[even:LAST, 0, :], x[t * P + even:N, :]).then_inc(x_tail, 16)
            sp.wait_ge(x_tail, 16)
            sp.dma_start(x_in[0:even, 0, :], x[t * P:t * P + even, :]).then_inc(x_loaded[0], 16)
            sp.dma_start(w_sb[:, :, :], w.rearrange("(k p) n -> p k n", p=P)).then_inc(w_loaded, 16)
            sp.wait_ge(etiles_ready, 1)
            sp.dma_start(tile_list.rearrange("(q b) -> q b", b=4), tile_i[:, :]).then_inc(tile_list_stored, 16)
            sp.wait_ge(tile_list_stored, 16)
            sp.dma_start(tile_row[:, 0:PAIRS], tile_list.rearrange("(q b) -> q b", q=1)).then_inc(tile_row_loaded, 16)

            sp.wait_ge(att_done, NT + XS)
            for j in range(XS):
                sp.wait_ge(xt_stored[j], 16 * (len(range(j, NT, XS)) + 1))

            def load_xt(t, j):
                sp.wait_ge(projected, t + 1)
                sp.dma_start(xt_in[:, j, :, :],
                             xln_t[bass.ds(t, 1), :, :].rearrange("a p n -> p (a n)").rearrange("p (k n) -> p k n", k=KT)
                             ).then_inc(xt_loaded[j], 16)

            def load_lows(c, j):
                sp.wait_ge(hot_ready, c - 1)
                for n in range(2):
                    sp.dma_start(lows_in[:, j, n, :],
                                 lows[n:n + 1, bass.ds(c * CE, CE)].partition_broadcast(P)).then_inc(lows_loaded[j], 16)

            load_xt(0, 0)
            load_xt(1, 1)
            sp.wait_ge(lows_ready, 1)
            for n in range(2):
                sp.dma_start(lows[n:n + 1, :].rearrange("a (q f) -> (a q) f", f=4 * P), low_rows[:, n, :]).then_inc(lows_stored, 16)
            sp.wait_ge(lows_stored, 32)
            for c in range(2):
                for n in range(2):
                    sp.dma_start(lows_in[:, c, n, :],
                                 lows[n:n + 1, c * CE:(c + 1) * CE].partition_broadcast(P)).then_inc(lows_loaded[c], 16)
            load_xt(2, 0)
            with sp.Fori(0, STEPS2) as i:
                for j in range(2):
                    load_lows(4 * i + 2 * j + 2, 0)
                    load_lows(4 * i + 2 * j + 3, 1)
                    load_xt(2 * i + j + 3, 1 - j)
            for t in range(2 * STEPS2 + 3, NT):
                load_xt(t, t % 2)

            for s, depth in ((pair_done, 2 * CH), (x12_ready, 2), (x12_stored, 32)):
                sp.sem_inc(s, depth)
            sp.wait_ge(xp_complete, 1)
            sp.wait_ge(weights_ready, 1)
            sp.dma_start(bias_b[:, :], bias.rearrange("(a n) -> a n", a=1).partition_broadcast(P)).then_inc(sums_loaded, 16)
            sp.dma_start(gate_b[:, :, :].rearrange("p e n -> p (e n)"),
                         gate_t.rearrange("(a e) n -> a (e n)", a=1).partition_broadcast(P)).then_inc(sums_loaded, 16)

            def load_own(t, full=True):
                sp.wait_ge(x12_ready, t + 1)
                at = bass.ds((t % 2) * D, D)
                if full:
                    sp.dma_start(x_own[:, at], tile_of(x, t)).then_inc(own_loaded, 16)
                else:
                    even = LAST // 16 * 16
                    sp.dma_start(x_own[even:LAST, at], x[t * P + even:N, :]).then_inc(own_tail, 16)
                    sp.wait_ge(own_tail, 16)
                    sp.dma_start(x_own[0:even, at], x[t * P:t * P + even, :]).then_inc(own_loaded, 16)
                sp.dma_start(xp_own[:, at], tile_of(xp, t)).then_inc(own_loaded, 16)
                sp.wait_ge(own_loaded, 32 * (t + 1))
                sp.nop().then_inc(sp_turn, 1)

            def store_x12(t):
                sp.wait_ge(x12_ready, t + 3)
                sp.dma_start(tile_of(x1_d, t), x1_sb[:, :]).then_inc(x12_stored, 16)
                sp.dma_start(tile_of(x2_d, t), x2_sb[:, :]).then_inc(x12_stored, 16)
                sp.wait_ge(x12_stored, 32 * (t + 1) + 32)
                sp.nop().then_inc(sp_turn, 1)

            load_own(0)
            with sp.Fori(0, NT - 2) as t:
                load_own(t + 1)
                store_x12(t)
            load_own(NT - 1, False)
            store_x12(NT - 2)
            store_x12(NT - 1)

            for s, depth in ((tokens_turned, 4), (tokens_ready, 2), (h_ready, 2), (h_taken, 2), (act_turned, 2),
                             (act_t_ready, 2), (y_ready, 2), (y_taken, 1), (mixed, 2),
                             *((q, 16) for q in y_stored + out_stored)):
                sp.sem_inc(s, depth)
            sp.wait_ge(phase2_done, 1)
            sp.dma_start(b1_b[:, :, :].rearrange("p e n -> p (e n)"),
                         b1.rearrange("(a e) n -> a (e n)", a=1).partition_broadcast(P)).then_inc(biases_loaded, 16)
            sp.dma_start(b2_b[:, :, :].rearrange("p e n -> p (e n)"),
                         b2.rearrange("(a e) n -> a (e n)", a=1).partition_broadcast(P)).then_inc(biases_loaded, 16)

            def load_expert(e):
                sp.dma_start(w1_sb[:, e % 2, :, :].rearrange("p k n -> p (k n)"),
                             w1[e].rearrange("p k n -> p (k n)")).then_inc(expert_loaded[e % 2], 16)
                sp.dma_start(w2_sb[:, e % 2, :, :].rearrange("p k n -> p (k n)"),
                             w2[e].rearrange("p k n -> p (k n)")).then_inc(expert_loaded[e % 2], 16)
                sp.wait_ge(expert_loaded[e % 2], 32 * (e // 2 + 1))
                sp.sem_inc(expert_seen, 1)

            for e in range(NE):
                if e == 2:
                    sp.wait_ge(lists_ready, 1)
                if e >= 2:
                    end = sp.value_load(expert_end[0:1, e - 2:e - 1], min_val=0, max_val=SLOTS)
                    sp.wait_ge(y_ready, end + 2)
                load_expert(e)
            sp.wait_ge(y_complete, 1)

            def load_x1(t, j):
                sp.wait_ge(mixed, t + 1)
                sp.dma_start(x1_in[:, j, :], tile_of(x1_d, t)).then_inc(x1_loaded[j], 16)

            def store_out(t, j):
                sp.wait_ge(mixed, t + 3)
                sp.dma_start(tile_of(out, t), out_sb[:, j, :]).then_inc(out_stored[j], 16)

            load_x1(0, 0)
            with sp.Fori(0, NT // 2) as i:
                for j in range(2):
                    load_x1(2 * i + j + 1, 1 - j)
                    store_out(2 * i + j, j)
            t, even = NT - 1, LAST // 16 * 16
            sp.wait_ge(mixed, NT + 2)
            sp.dma_start(out[t * P:t * P + even, :], out_sb[0:even, 0, :]).then_inc(out_stored[0], 16)
            sp.dma_start(out[t * P + even:N, :], out_sb[even:LAST, 0, :]).then_inc(out_stored[0], 16)
            sp.wait_ge(out_stored[0], 16 * (NT // 2 + 3))
            sp.wait_ge(out_stored[1], 16 * (NT // 2 + 1))

        @block.gpsimd
        def _(pool):
            pool.iota(iota[:, :], [[1, P]], base=0, channel_multiplier=0,
                      allow_small_or_imprecise_dtypes=True).then_inc(consts, 1)
            pool.iota(lane[:, :], [[1, 1]], base=0, channel_multiplier=1,
                      allow_small_or_imprecise_dtypes=True).then_inc(consts, 1)
            pool.iota(pair_id[:, :], [[1, 4]], base=0, channel_multiplier=4,
                      allow_small_or_imprecise_dtypes=True).then_inc(consts, 1)
            pool.wait_ge(cleared, 4)
            pool.affine_select(out=ident[:, :], in_=ident[:, :], compare_op=ALU.not_equal, fill=1.0,
                               base=0, pattern=[[-1, P]], channel_multiplier=1).then_inc(consts, 1)
            pool.affine_select(out=upper[:, :], in_=upper[:, :], compare_op=ALU.is_ge, fill=1.0,
                               base=0, pattern=[[-1, P]], channel_multiplier=1).then_inc(consts, 1)
            pool.wait_ge(etiles_ready, 1)
            pool.wait_ge(tiles_stored, 32)
            for n, tiles in enumerate((src_tiles, dst_tiles)):
                for b in range(4):
                    pool.indirect_dma_start(pair_rows[:, n, b * P:(b + 1) * P], None, tiles,
                                            bass.IndirectOffsetOnAxis(etile_i[:, b:b + 1], 0)).then_inc(pairs_gathered, 16)

            pool.wait_ge(xp_complete, 1)
            pool.wait_ge(weights_ready, 1)
            with pool.Fori(0, NCH) as i:
                for h in range(CH // GR):
                    pool.tensor_copy(message_idx[:, h * GR:(h + 1) * GR],
                                     pair_src[:, bass.ds(i * CH + h * GR, GR)]).then_inc(idx_copied, 1)
                    pool.wait_ge(idx_copied, i * (CH // GR) + h + 1)
                    for j in range(GR):
                        pool.wait_ge(pair_done, i * CH + h * GR + j + 1 + 2 * CH - GR)
                        pool.nop().then_inc(pool_turn, 1)
                        pool.indirect_dma_start(messages[:, j, :], None, xp, bass.IndirectOffsetOnAxis(
                            message_idx[:, h * GR + j:h * GR + j + 1], 0)).then_inc(message_loaded[j], 16)

            pool.wait_ge(ids_ready, 1)
            with pool.Fori(0, SLOTS // 8) as i:
                for g in range(2):
                    pool.tensor_copy(idx_ring[:, 4 * g:4 * g + 4], token_idx[:, bass.ds(8 * i + 4 * g, 4)]).then_inc(idx3, 1)
                    pool.wait_ge(idx3, 2 * i + g + 1)
                    for j in range(4):
                        pool.wait_ge(tokens_turned, 8 * i + 4 * g + j + 1)
                        pool.nop().then_inc(pool_turn, 1)
                        pool.indirect_dma_start(tokens_in[:, j, :], None, x2_d, bass.IndirectOffsetOnAxis(
                            idx_ring[:, 4 * g + j:4 * g + j + 1], 0)).then_inc(tokens_loaded[j], 16)
            pool.wait_ge(y_complete, 1)

            def fetch_results(t, j, n):
                pool.wait_ge(mixed, t + 1)
                pool.tensor_copy(idx_ring[:, 2 * j:2 * j + 2], slots_i[:, bass.ds(t, 1), :].rearrange("p a c -> p (a c)")).then_inc(idx3, 1)
                pool.wait_ge(idx3, SLOTS // 4 + 1 + t)
                pool.nop().then_inc(pool_turn, 1)
                for n, rows in enumerate((y_first, y_second)):
                    pool.indirect_dma_start(rows[:, j, :], None, y_d, bass.IndirectOffsetOnAxis(
                        idx_ring[:, 2 * j + n:2 * j + n + 1], 0)).then_inc(first_loaded[j], 16)

            with pool.Fori(0, NT // 2) as i:
                for j in range(2):
                    fetch_results(2 * i + j, j, i)
            fetch_results(NT - 1, 0, NT // 2)

        @block.scalar
        def _(act):
            def root(t, j):
                act.wait_ge(stats_ready, t + 1)
                act.activation(std[:, j, :], mv[:, j, 1:2], ACT.Sqrt, bias=eps_col[:, :]).then_inc(std_ready, 1)

            def evacuate(t, j, k, r):
                act.wait_ge(turned, t + 3)
                act.wait_ge(xt_stored[j], 16 * r + 16)
                act.wait_ge(att_done, t + 1)
                act.activation(xt_out[:, j, :, :].rearrange("p k n -> p (k n)"),
                               ps[:, 2 * k:2 * k + 2, :].rearrange("p b n -> p (b n)"), ACT.Copy).then_inc(xt_evacuated, 1)
                act.wait_ge(xt_evacuated, t + 3)
                act.dma_start(xln_t[bass.ds(t, 1), :, :].rearrange("a p n -> p (a n)"),
                              xt_out[:, j, :, :].rearrange("p k n -> p (k n)")).then_inc(xt_stored[j], 16)

            act.wait_ge(cleared, 4)
            root(0, 0)
            with act.Fori(0, HALF) as i:
                for j in range(XS):
                    root(i * XS + j + 1, (j + 1) % XS)
                    evacuate(i * XS + j, j, j % 2, i)
            evacuate(NT - 1, 0, 0, HALF)

            def take_xp(t, j, r):
                act.wait_ge(projected, t + 3)
                act.wait_ge(xp_stored[j], 16 * r + 16)
                act.activation(xp_out[:, j, :], ps[:, 2 * j:2 * j + 2, :].rearrange("p b n -> p (b n)"),
                               ACT.Copy).then_inc(xp_evacuated, 1)
                act.wait_ge(xp_evacuated, t + 3)
                act.dma_start(tile_of(xp, t), xp_out[:, j, :]).then_inc(xp_stored[j], 16)

            def take_dst(c, j):
                act.wait_ge(dst_fetched, c + 3)
                act.activation(dst_col[:, bass.ds(c * CH, CH), :].rearrange("p c h -> p (c h)"),
                               ps[:, 6 + j, 0:2 * H * CH], ACT.Copy).then_inc(dst_taken, 1)

            act.wait_ge(att_done, NT + XS)
            take_xp(0, 0, 0)
            take_xp(1, 1, 0)
            with act.Fori(0, STEPS2) as i:
                for j in range(2):
                    take_xp(2 * i + j + 2, j, i + 1)
                    take_dst(4 * i + 2 * j, 0)
                    take_dst(4 * i + 2 * j + 1, 1)
            t = 2 * STEPS2 + 2
            take_xp(t, 0, t // 2)
            take_dst(NCH - 2, 0)
            take_dst(NCH - 1, 1)
            t += 1
            take_xp(t, 1, t // 2)
            act.wait_ge(as_turned, 1)
            act.activation(as_rows[:, :, :].rearrange("q h f -> q (h f)"),
                           ps[0:PQ, 4:8, :].rearrange("q h f -> q (h f)"), ACT.Copy).then_inc(as_rows_ready, 1)
            for t in range(t + 1, t + 3):
                take_xp(t, t % 2, t // 2)
            t0 = t + 1
            for t in range(t0, t0 + 3):
                take_xp(t, t % 2, t // 2)
            act.wait_ge(z_ready, 1)
            act.activation(pair_cols[:, :, 0:H], z_col[:, 0, :, :], ACT.Exp).then_inc(exp_ready, 1)
            act.activation(z_col[:, 2, :, :], z_col[:, 1, :, :], ACT.Exp).then_inc(exp_ready, 1)
            t0 = t + 1
            for t in range(t0, NT):
                take_xp(t, t % 2, t // 2)
            for j in range(2):
                act.wait_ge(xp_stored[j], 16 * (len(range(j, NT, 2)) + 1))
            act.nop().then_inc(xp_complete, 1)

            act.wait_ge(weights_ready, 1)
            act.wait_ge(xp_complete, 1)
            with act.Fori(0, NCH) as i:
                act.wait_ge(hot_built, i + 1)
                half = i % 2
                for j in range(CH):
                    act.wait_ge(pair_done, i * CH + j + 1 + 2 * CH - GR)
                    for h in range(H):
                        last = act.activation(weighted[:, j % GR, h, :],
                                              dst_hot[:, bass.ds(half * CH + j, 1), :].rearrange("p a n -> p (a n)"),
                                              ACT.Copy, scale=pair_cols[:, bass.ds(i * CH + j, 1), h])
                    last.then_inc(weighted_ready, 1)

            act.wait_ge(gaps_ready, 1)
            act.activation(e_gap[:, :], gap[:, :], ACT.Exp).then_inc(gap_exp, 1)

            def take_tokens(s, j):
                act.wait_ge(tokens_turned, s + 5)
                act.wait_ge(h_ready, s + 1)
                act.activation(tokens_t[:, j, :, :].rearrange("p k n -> p (k n)"),
                               ps[:, 0:2, :].rearrange("p b n -> p (b n)"), ACT.Copy).then_inc(tokens_ready, 1)

            def sigmoid(s, j):
                act.wait_ge(g_ready, s + 1)
                act.activation(sig_sb[:, j, :], g_sb[:, j, :], ACT.Sigmoid, scale=ALPHA).then_inc(sig_ready, 1)

            def take_act(s, j):
                act.wait_ge(act_turned, s + 3)
                act.wait_ge(y_ready, s + 1)
                act.activation(act_t[:, j, :, :].rearrange("p k n -> p (k n)"), ps[:, 4, 0:FT * P], ACT.Copy).then_inc(act_t_ready, 1)

            def store_y(s, j):
                act.wait_ge(y_taken, s + 2)
                act.dma_start(tile_of(y_d, s), y_sb[:, j, :]).then_inc(y_stored[j], 16)

            take_tokens(0, 0)
            take_tokens(1, 1)
            sigmoid(0, 0)
            sigmoid(1, 1)
            take_act(0, 0)
            take_tokens(2, 0)
            with act.Fori(0, SLOTS // 2 - 2) as i:
                for j in range(2):
                    s = 2 * i + j + 2
                    sigmoid(s, j)
                    take_act(s - 1, 1 - j)
                    take_tokens(s + 1, 1 - j)
                    store_y(s - 2, j)
            sigmoid(SLOTS - 2, 0)
            take_act(SLOTS - 3, 1)
            take_tokens(SLOTS - 1, 1)
            store_y(SLOTS - 4, 0)
            sigmoid(SLOTS - 1, 1)
            take_act(SLOTS - 2, 0)
            store_y(SLOTS - 3, 1)
            take_act(SLOTS - 1, 1)
            store_y(SLOTS - 2, 0)
            store_y(SLOTS - 1, 1)
            for j in range(2):
                act.wait_ge(y_stored[j], 16 * (SLOTS // 2 + 1))
            act.nop().then_inc(y_complete, 1)

        @block.vector
        def _(v):
            step = Steps(v, dve)
            v.memset(rows_in[:, 0, :], 0).then_inc(cleared, 1)
            v.memset(rows_in[:, 1, :], NT * P).then_inc(cleared, 1)
            v.memset(ident[:, :], 0.0).then_inc(cleared, 1)
            v.memset(eps_col[:, :], EPS)
            v.memset(zero_col[:, :], 0.0)
            v.memset(ones[:, :], 1.0)
            v.memset(att_blk[:, :, :], 0.0)
            v.memset(differs[:, :], 0.0)
            v.memset(start_all[:, :], 0.0)
            v.memset(tile_row[:, PAIRS:PAIRS + 1], NT)
            v.memset(joins[:, :], 0.0)
            v.memset(carry_t[:, :, :], -BIG)
            v.memset(upper[:, :], 0.0).then_inc(cleared, 1)
            v.wait_ge(rows_loaded, 96)
            step.then(v.tensor_copy(dst_f[:, :], rows_in[:, 1, :]))
            for t in range(1, NT):
                step.then(v.tensor_scalar(below[:, :], dst_f[:, :], float(t * P), 0.0, ALU.is_lt, ALU.add,
                                          accum_out=count_part[:, t - 1:t]))
            v.nop().then_inc(counted, 1)
            v.wait_ge(att_loaded, 32)
            for h in range(H):
                for n in range(2):
                    last = v.tensor_copy(att_blk[:, 2 * h:2 * h + 2, n * H + h], att_in[:, n, 2 * h:2 * h + 2])
            last.then_inc(att_placed, 1)
            v.wait_ge(counts_summed, 1)
            v.wait_ge(consts, 3)
            step.then(v.tensor_copy(count_i[:, 0, :], ps[:, 5, 0:NT - 1]))
            step.then(v.tensor_scalar(count_i[:, 1, :], count_i[:, 0, :], 7, None, ALU.logical_shift_right))
            step.then(v.tensor_copy(start_f[:, :], count_i[:, 1, :]))
            step.then(v.tensor_tensor(start_f[:, :], start_f[:, :], iota[:, 1:NT], ALU.add))
            for b in range(4):
                step.then(v.tensor_scalar(reached[:, :], start_f[0:PQ, :], pair_id[:, b:b + 1], 0.0,
                                          ALU.is_le, ALU.add, accum_out=tile_f[:, b:b + 1]))
            step.then(v.tensor_scalar(minus_base[:, :], tile_f[:, :], float(-P), None, ALU.mult))
            step.then(v.tensor_copy(start_all[:, 1:NT], start_f[0:1, :]))
            step.then(v.memset(start_all[:, NT:NT + 1], float(PAIRS)))
            v.tensor_copy(start_row[:, :], start_all[:, :])
            v.tensor_copy(tile_i[:, :], tile_f[:, :])
            v.tensor_tensor(etile_i[:, :], pair_id[:, :], tile_f[:, :], ALU.subtract).then_inc(etiles_ready, 1)

            def w_att_copy():
                v.wait_ge(w_att_summed, 1)
                v.tensor_copy(w_att[:, :, :].rearrange("p k m -> p (k m)"), ps[:, 6, 0:2 * H * KT]).then_inc(w_att_ready, 1)

            def measure(j, r):
                v.wait_ge(x_loaded[j], 16 * r + 16)
                v.bn_stats(stats[:, j, 0, :], x_in[:, j, 0:D // 2])
                step.then(v.bn_stats(stats[:, j, 1, :], x_in[:, j, D // 2:D]))

            def invert(t, j):
                v.wait_ge(std_ready, t + 1)
                return v.reciprocal(rstd[:, j, :], std[:, j, :])

            def combine(j):
                v.bn_aggr(mv[:, j, :], stats[:, j, :, :].rearrange("p a b -> p (a b)")).then_inc(stats_ready, 1)

            def normalise(t, j, k):
                v.wait_ge(turned, t + 1)
                v.tensor_scalar(xln[:, k, :], x_in[:, j, :], mv[:, j, 0:1], rstd[:, j, :],
                                ALU.subtract, ALU.mult).then_inc(xln_ready, 1)

            measure(0, 0)
            combine(0)
            w_att_copy()
            with v.Fori(0, HALF) as i:
                step.rounds(i, 2 * XS)
                for j in range(XS):
                    nxt = (j + 1) % XS
                    measure(nxt, i + (j + 1) // XS)
                    step.mark(invert(i * XS + j, j))
                    combine(nxt)
                    step.wait()
                    normalise(i * XS + j, j, j % 2)
            step.end_rounds(HALF)
            step.then(invert(NT - 1, 0))
            normalise(NT - 1, 0, 0)

            v.wait_ge(pairs_gathered, 128)
            v.tensor_scalar(int_rows[:, 0, :], pair_rows[:, 0, :], P - 1, None, ALU.bitwise_and)
            v.tensor_scalar(int_rows[:, 1, :], pair_rows[:, 0, :], 7, None, ALU.logical_shift_right)
            v.tensor_copy(src_rows[:, :], pair_rows[:, 0, :])
            step.then(v.tensor_copy(dst_rows[:, :], pair_rows[:, 1, :]))
            for b in range(4):
                last = v.tensor_scalar(rel_rows[:, b * P:(b + 1) * P], dst_rows[:, b * P:(b + 1) * P],
                                       minus_base[:, b:b + 1], None, ALU.add)
            v.tensor_copy(low_rows[:, 0, :], int_rows[:, 0, :])
            step.then(v.tensor_copy(hi_rows[:, :], int_rows[:, 1, :]))
            v.tensor_copy(low_rows[:, 1, :], rel_rows[:, :]).then_inc(lows_ready, 1)
            v.nop().then_inc(rows_ready, 1)

            v.wait_ge(att_done, NT + XS)
            step.then(v.tensor_copy(node_att[:, :, :].rearrange("p t m -> p (t m)"), ps[:, 4, 0:NT * 2 * H]))
            step.then(v.tensor_copy(node_parts[:, 0, :, :], node_att[:, :, :]))
            step.then(v.tensor_tensor(node_res[:, 0, :, :], node_att[:, :, :], node_parts[:, 0, :, :], ALU.subtract))
            step.then(v.tensor_copy(node_parts[:, 1, :, :], node_res[:, 0, :, :]))
            step.then(v.tensor_tensor(node_res[:, 1, :, :], node_res[:, 0, :, :], node_parts[:, 1, :, :], ALU.subtract))
            v.tensor_copy(node_parts[:, 2, :, :], node_res[:, 1, :, :]).then_inc(parts_ready, 1)

            def by_pair(ap):
                return ap.rearrange("p (q b) -> p b q", b=4)

            v.wait_ge(rows_turned, 1)
            turned_rows = [ps[:, 4 + n, 0:PAIRS].rearrange("p (b q) -> p b q", b=4) for n in range(3)]
            step.then(v.tensor_copy(by_pair(hi_col[:, :]), turned_rows[0]))
            v.tensor_copy(by_pair(pair_src[:, :]), turned_rows[1])
            v.tensor_copy(by_pair(pair_dst[:, :]), turned_rows[2]).then_inc(cols_taken, 1)
            step.then(v.tensor_tensor(hi_hot[:, :, :], hi_col[:, :].unsqueeze(2).to_broadcast([P, PAIRS, NT]),
                                      iota[:, 0:NT].unsqueeze(1).to_broadcast([P, PAIRS, NT]), ALU.is_equal))

            def compare(c, j, r):
                v.wait_ge(lows_loaded[j], 32 * r + 32)
                v.wait_ge(dst_fetched, c + 1)
                v.tensor_scalar(lows_hot[:, j, :, :].rearrange("p a b -> p (a b)"),
                                lows_in[:, j, :, :].rearrange("p a b -> p (a b)"),
                                lane[:, :], None, ALU.is_equal).then_inc(hot_ready, 1)

            def pick(c):
                for g in range(4):
                    v.wait_ge(src_fetched, 4 * c + g + 1)
                    ins = v.tensor_tensor(
                        picked[:, g % 2, :, :, :].rearrange("p a t h -> p (a t) h"),
                        ps[:, 4 + g % 2, 0:4 * NT * H].rearrange("p (t h) -> p t h", h=H),
                        hi_hot[:, bass.ds(c * CH + 4 * g, 4), :].rearrange("p a t -> p (a t)").unsqueeze(2)
                        .to_broadcast([P, 4 * NT, H]), ALU.mult)
                    ins.then_inc(src_taken, 1)
                    v.wait_ge(src_taken, 4 * c + g + 3)
                    last = v.tensor_reduce(as_col[:, bass.ds(c * CH + 4 * g, 4), :],
                                           picked[:, g % 2, :, :, :].rearrange("p a t h -> p a h t"), AX.X, ALU.add)
                    if g % 2:
                        step.then(last)

            compare(0, 0, 0)
            with v.Fori(0, NCH // 2 - 1) as i:
                step.rounds(i, 4)
                compare(2 * i + 1, 1, i)
                pick(2 * i)
                compare(2 * i + 2, 0, i + 1)
                pick(2 * i + 1)
            step.end_rounds(NCH // 2 - 1)
            compare(NCH - 1, 1, NCH // 2 - 1)
            pick(NCH - 2)
            pick(NCH - 1)
            v.nop().then_inc(as_ready, 1)

            step.then(v.tensor_scalar(valid[:, :], rel_rows[:, :], 0.0, None, ALU.is_ge))
            step.then(v.scalar_tensor_tensor(out=valid[:, :], in0=rel_rows[:, :], scalar=P - 0.5, in1=valid[:, :],
                                             op0=ALU.is_lt, op1=ALU.mult))
            step.then(v.scalar_tensor_tensor(out=key[:, :], in0=dst_rows[:, :], scalar=1.0, in1=valid[:, :],
                                             op0=ALU.add, op1=ALU.mult))
            step.then(v.tensor_tensor(differs[:, 1:4 * P], key[:, 1:4 * P], key[:, 0:4 * P - 1], ALU.not_equal))
            step.then(v.tensor_scalar(reset[:, :], differs[:, :], -BIG, None, ALU.mult))
            v.wait_ge(as_rows_ready, 1)
            F4 = 4 * P

            def scans(first):
                for h in range(H):
                    a = -BIG if first else carry[:, 0, h:h + 1]
                    b = -BIG if first else carry[:, 1, h:h + 1]
                    v.tensor_tensor_scan(fwd[:, h, :], reset[:, 0:F4], as_rows[:, h, :], a, ALU.add, ALU.max)
                    last = v.tensor_tensor_scan(bwd[:, h, ::-1], reset[:, 1:F4 + 1][:, ::-1], as_rows[:, h, ::-1], b,
                                                ALU.add, ALU.max)
                step.then(last)

            scans(True)
            v.tensor_copy(ends[:, 0, :], fwd[:, :, F4 - 1])
            v.tensor_copy(ends[:, 1, :], bwd[:, :, 0])
            v.tensor_copy(ends[:, 2, :], key[:, 0:1].to_broadcast([PQ, H]))
            v.tensor_copy(ends[:, 3, :], key[:, F4 - 1:F4].to_broadcast([PQ, H])).then_inc(ends_ready, 1)
            v.wait_ge(ends_turned, 1)
            step.then(v.tensor_copy(ends_t[:, :, :].rearrange("h a q -> h (a q)"), ps[0:H, 4, 0:4 * PQ]))
            step.then(v.tensor_tensor(joins[:, 1:PQ], ends_t[:, 2, 1:PQ], ends_t[:, 3, 0:PQ - 1], ALU.is_equal))
            step.then(v.tensor_tensor(whole[:, :], ends_t[:, 2, :], ends_t[:, 3, :], ALU.is_equal))
            v.tensor_tensor(chain[:, 0, :], whole[:, :], joins[:, 0:PQ], ALU.mult)
            step.then(v.tensor_tensor(chain[:, 1, :], whole[:, :], joins[:, 1:PQ + 1], ALU.mult))
            step.then(v.tensor_scalar(chain[:, :, :], chain[:, :, :], 1.0, BIG, ALU.subtract, ALU.mult))
            v.tensor_tensor_scan(scan_t[:, 0, :], chain[:, 0, :], ends_t[:, 0, :], -BIG, ALU.add, ALU.max)
            step.then(v.tensor_tensor_scan(scan_t[:, 1, ::-1], chain[:, 1, ::-1], ends_t[:, 1, ::-1], -BIG, ALU.add, ALU.max))
            step.then(v.tensor_scalar(whole[:, :], joins[:, 0:PQ], 1.0, BIG, ALU.subtract, ALU.mult))
            step.then(v.tensor_tensor(carry_t[:, 0, 1:PQ], scan_t[:, 0, 0:PQ - 1], whole[:, 1:PQ], ALU.add))
            step.then(v.tensor_tensor(carry_t[:, 1, 0:PQ - 1], scan_t[:, 1, 1:PQ], whole[:, 1:PQ], ALU.add))
            v.tensor_copy(carry_t[:, 2, :], joins[:, 1:PQ + 1]).then_inc(carry_ready, 1)
            v.wait_ge(carry_turned, 1)
            step.then(v.tensor_copy(carry[:, :, :].rearrange("q a h -> q (a h)"), ps[0:PQ, 5, 0:3 * H]))
            scans(False)
            v.tensor_tensor(as_rows[:, :, :], fwd[:, :, :], bwd[:, :, :], ALU.max)
            step.then(v.tensor_scalar(differs[:, F4:F4 + 1], carry[:, 2, 0:1], -1.0, 1.0, ALU.mult, ALU.add))
            v.tensor_tensor(last_rows[:, :], differs[:, 1:F4 + 1], valid[:, :], ALU.mult).then_inc(max_ready, 1)
            v.wait_ge(max_turned, 1)
            for h in range(H):
                v.tensor_copy(max_col[:, :, h].rearrange("p (q b) -> p b q", b=4),
                              ps[:, 4 + h, 0:PAIRS].rearrange("p (b q) -> p b q", b=4)).then_inc(max_taken, 1)
            v.wait_ge(max_turned, 2)
            step.then(v.tensor_copy(by_pair(last_col[:, :]), ps[:, 4, 0:PAIRS].rearrange("p (b q) -> p b q", b=4)))
            a_s, a_d = dst_col[:, :, 0:H], dst_col[:, :, H:2 * H]
            step.then(v.tensor_tensor(max_col[:, :, :], max_col[:, :, :], a_s, ALU.max))
            v.tensor_tensor(z_col[:, 2, :, :], max_col[:, :, :], a_d, ALU.add)
            v.tensor_tensor(z_col[:, 0, :, :], as_col[:, :, :], a_d, ALU.add)
            step.then(v.tensor_tensor(z_col[:, 1, :, :], a_s, a_d, ALU.add))
            for n in range(3):
                last = v.scalar_tensor_tensor(out=z_col[:, n, :, :], in0=z_col[:, n, :, :], scalar=NEG_SLOPE,
                                              in1=z_col[:, n, :, :], op0=ALU.mult, op1=ALU.max)
            step.then(last)
            for n in range(2):
                last = v.tensor_tensor(z_col[:, n, :, :], z_col[:, n, :, :], z_col[:, 2, :, :], ALU.subtract)
            last.then_inc(z_ready, 1)
            v.wait_ge(exp_ready, 2)
            v.tensor_tensor(pair_cols[:, :, H:2 * H], z_col[:, 2, :, :],
                            last_col[:, :].unsqueeze(2).to_broadcast([P, PAIRS, H]), ALU.mult)
            v.tensor_copy(pair_cols[:, :, 2 * H], last_col[:, :]).then_inc(weights_ready, 1)

            v.wait_ge(xp_complete, 1)
            v.memset(ps[:, 0:2, :], 0.0)
            v.memset(ps[:, 4, 0:NCOL], 0.0).then_inc(acc_free, 1)
            v.memset(ps[:, 2:4, :], 0.0)
            v.memset(ps[:, 5, 0:NCOL], 0.0).then_inc(acc_free, 1)

            def build_hot(b):
                v.wait_ge(pair_done, b * CH + CH)
                v.tensor_tensor(dst_hot[:, bass.ds((b % 2) * CH, CH), :],
                                pair_dst[:, bass.ds(b * CH, CH)].unsqueeze(2).to_broadcast([P, CH, P]),
                                iota[:, :].unsqueeze(1).to_broadcast([P, CH, P]), ALU.is_equal).then_inc(hot_built, 1)

            ROUND = 39

            def finish(t):
                step = Steps(v, epi)
                step.rounds(t, ROUND)
                half = t % 2
                end = v.value_load(start_row[0:1, bass.ds(t + 1, 1)], min_val=1, max_val=PAIRS)
                v.wait_ge(pair_done, end + 2 * CH)
                step.then(v.tensor_scalar(sums[:, :], ps[:, bass.ds(half + 4, 1), 0:NCOL].rearrange("p a n -> p (a n)"),
                                          1.0, None, ALU.mult))
                step.then(v.tensor_scalar(no_edge[:, :], sums[:, 2 * H:NCOL], -1.0, 1.0, ALU.mult, ALU.add))
                step.then(v.tensor_scalar(own_w[:, :], sums[:, H:2 * H], no_edge[:, :], None, ALU.add))
                step.then(v.tensor_tensor(total[:, :], own_w[:, :], sums[:, 0:H], ALU.add))
                step.then(v.reciprocal(inv_total[:, :], total[:, :]))
                step.then(v.tensor_tensor(own_share[:, :], own_w[:, :], inv_total[:, :], ALU.mult))
                v.wait_ge(own_loaded, 32 * (t + 1))
                at = half * D
                for h in range(H):
                    last = v.scalar_tensor_tensor(
                        out=summed[:, h * C:(h + 1) * C], in0=xp_own[:, bass.ds(at + h * C, C)],
                        scalar=own_share[:, h:h + 1], in1=bias_b[:, h * C:(h + 1) * C], op0=ALU.mult, op1=ALU.add)
                step.then(last)
                acc = ps[:, bass.ds(half * 2, 2), :].rearrange("p b n -> p (b n)")
                for h in range(H):
                    last = v.scalar_tensor_tensor(
                        out=summed[:, h * C:(h + 1) * C], in0=acc[:, h * C:(h + 1) * C],
                        scalar=inv_total[:, h:h + 1], in1=summed[:, h * C:(h + 1) * C], op0=ALU.mult, op1=ALU.add)
                step.then(last)
                v.tensor_scalar(acc, zero_col[:, :].to_broadcast([P, D]), 1.0, None, ALU.mult)
                v.tensor_copy(ps[:, bass.ds(half + 4, 1), 0:NCOL].rearrange("p a n -> p (a n)"),
                              zero_col[:, :].to_broadcast([P, NCOL])).then_inc(acc_free, 1)
                v.wait_ge(x12_stored, 32 * (t + 1))
                x1_t, x2_t = x1_sb[:, :], x2_sb[:, :]
                step.then(v.scalar_tensor_tensor(out=x1_t, in0=summed[:, :], scalar=0.0, in1=x_own[:, bass.ds(at, D)],
                                                 op0=ALU.max, op1=ALU.add))
                v.bn_stats(stats2[:, 0, :], x1_sb[:, 0:D // 2])
                step.then(v.bn_stats(stats2[:, 1, :], x1_sb[:, D // 2:D]))
                step.mark(v.memset(var2[:, :], 0.0))
                step.mark(v.bn_aggr(mv2[:, :], stats2[:, :, :].rearrange("p a b -> p (a b)")))
                step.wait()
                step.then(v.tensor_scalar(var2[:, :], mv2[:, 1:2], EPS, None, ALU.add))
                step.then(v.tensor_scalar(guess_i[:, :], var2[:, :].bitcast(I32), 1, None, ALU.logical_shift_right))
                step.then(v.tensor_scalar(guess_i[:, :], guess_i[:, :], -1.0, float(0x5F3759DF), ALU.mult, ALU.add))
                step.then(v.tensor_scalar(half2[:, :], var2[:, :], -0.5, None, ALU.mult))
                step.then(v.tensor_copy(root2[:, :], guess_i[:, :].bitcast(F32)))
                for _ in range(4):
                    step.then(v.tensor_tensor(square2[:, :], root2[:, :], root2[:, :], ALU.mult))
                    step.then(v.tensor_scalar(square2[:, :], square2[:, :], half2[:, :], 1.5, ALU.mult, ALU.add))
                    if _ < 3:
                        step.then(v.tensor_tensor(root2[:, :], root2[:, :], square2[:, :], ALU.mult))
                step.then(v.tensor_tensor(root2[:, :], root2[:, :], square2[:, :], ALU.mult))
                step.then(v.tensor_scalar(x2_t, x1_t, mv2[:, 0:1], root2[:, :], ALU.subtract, ALU.mult))
                for e in range(NE):
                    step.then(v.tensor_tensor_reduce(product[:, :], x2_t, gate_b[:, e, :], 1.0, 0.0, ALU.mult, ALU.add,
                                                     gate_now[:, e:e + 1]))
                step.then(v.tensor_scalar(gate_all[:, bass.ds(t, 1), :].rearrange("p a e -> p (a e)"), gate_now[:, :],
                                          1.0, None, ALU.mult))
                v.nop().then_inc(x12_ready, 1)
                assert step.n == ROUND, step.n

            def finish_until(b):
                lo = v.value_load(tile_row[0:1, bass.ds((b - 1) * CH, 1)], min_val=0, max_val=NT)
                hi = v.value_load(tile_row[0:1, bass.ds(b * CH, 1)], min_val=0, max_val=NT)
                with v.If(lo < hi):
                    with v.Fori(lo, hi) as t:
                        finish(t)

            v.wait_ge(sums_loaded, 32)
            build_hot(0)
            with v.Fori(1, NCH) as b:
                build_hot(b)
                finish_until(b)
            finish_until(NCH)
            v.wait_ge(x12_stored, 32 * NT + 32)
            v.nop().then_inc(phase2_done, 1)

            step = Steps(v, dve3)
            step.then(v.tensor_scalar(reversed_e[:, :], iota[:, 0:NE], -1.0, float(NE), ALU.mult, ALU.add))
            gates = gate_all
            for c in range(2):
                step.then(v.tensor_reduce(best[:, c, :], gates[:, :, :], AX.X, ALU.max))
                step.then(v.tensor_tensor(is_best[:, :, :], gates[:, :, :], best[:, c, :].unsqueeze(2).to_broadcast([P, NT, NE]), ALU.is_equal))
                step.then(v.tensor_tensor(rank[:, :, :], is_best[:, :, :], reversed_e[:, :].unsqueeze(1).to_broadcast([P, NT, NE]), ALU.mult))
                step.then(v.tensor_reduce(rank_best[:, :], rank[:, :, :], AX.X, ALU.max))
                step.then(v.tensor_tensor(chosen[:, c, :, :], reversed_e[:, :].unsqueeze(1).to_broadcast([P, NT, NE]),
                                          rank_best[:, :].unsqueeze(2).to_broadcast([P, NT, NE]), ALU.is_equal))
                if c == 0:
                    step.then(v.scalar_tensor_tensor(out=gate_rest[:, :, :], in0=chosen[:, 0, :, :], scalar=-BIG,
                                                     in1=gates[:, :, :], op0=ALU.mult, op1=ALU.add))
                    gates = gate_rest
            v.tensor_tensor(gap[:, :], best[:, 1, :], best[:, 0, :], ALU.subtract).then_inc(gaps_ready, 1)
            step.then(v.tensor_tensor(selected[:, :, :], chosen[:, 0, :, :], chosen[:, 1, :, :], ALU.add))
            step.then(v.tensor_scalar(real_node[:, :], lane[:, :], float(LAST), None, ALU.is_lt))
            step.then(v.tensor_scalar(far[:, :], lane[:, :], float(LAST), float(1 << 20), ALU.is_ge, ALU.mult))
            v.tensor_scalar(selected[:, NT - 1, :], selected[:, NT - 1, :], real_node[:, :], None, ALU.mult).then_inc(selected_ready, 1)
            v.memset(goes_on[:, :, :], 1.0)
            step.then(v.tensor_copy(token_id[:, :, :], iota[:, 0:NT].unsqueeze(2).to_broadcast([P, NT, 2])))
            step.then(v.memset(goes_on[:, :, 0:1], 0.0))
            step.then(v.tensor_scalar(token_id[:, :, :], token_id[:, :, :], float(P), lane[:, :], ALU.mult, ALU.add))
            v.wait_ge(ranks_summed, 1)
            step.then(v.tensor_copy(per_tile[:, :, :].rearrange("p e t -> p t e"), ps[:, 1, 0:NT * NE].rearrange("p (t e) -> p t e", e=NE)))
            step.then(v.tensor_tensor_scan(so_far[:, :, :].rearrange("p e t -> p (e t)"), goes_on[:, :, :].rearrange("p e t -> p (e t)"),
                                           per_tile[:, :, :].rearrange("p e t -> p (e t)"), 0.0, ALU.mult, ALU.add))
            step.then(v.tensor_scalar(count_e[:, :], so_far[:, :, NT - 1], float(P - 1), None, ALU.add))
            step.then(v.tensor_copy(tiles_ei[:, 0, :], count_e[:, :]))
            step.then(v.tensor_scalar(tiles_ei[:, 1, :], tiles_ei[:, 0, :], 7, None, ALU.logical_shift_right))
            step.then(v.tensor_copy(tiles_e[:, :], tiles_ei[:, 1, :]))
            step.then(v.tensor_tensor_scan(ends_e[:, :], ones[:, 0:NE], tiles_e[:, :], 0.0, ALU.mult, ALU.add))
            v.tensor_copy(expert_end[:, :], ends_e[0:1, :])
            step.then(v.tensor_tensor(first_slot[:, :], ends_e[:, :], tiles_e[:, :], ALU.subtract))
            step.then(v.tensor_scalar(first_slot[:, :], first_slot[:, :], float(P), None, ALU.mult))
            step.then(v.tensor_tensor(at_end[:, :, :], ends_e[0:1, :].unsqueeze(1).to_broadcast([1, SLOTS, NE]),
                                      iota[0:1, 0:SLOTS].unsqueeze(2).to_broadcast([1, SLOTS, NE]), ALU.is_le))
            step.then(v.tensor_reduce(expert_f[:, :], at_end[:, :, :], AX.X, ALU.add))
            v.tensor_scalar(expert_row[:, :], expert_f[:, :], float(NE - 1), None, ALU.min).then_inc(lists_ready, 1)
            step.then(v.tensor_tensor(per_tile[:, :, :], so_far[:, :, :], per_tile[:, :, :], ALU.subtract))
            step.then(v.tensor_tensor(per_tile[:, :, :], per_tile[:, :, :], first_slot[:, :].unsqueeze(2).to_broadcast([P, NE, NT]), ALU.add))
            step.then(v.tensor_tensor(position[:, :, :], ps[:, 0, 0:NT * NE].rearrange("p (t e) -> p t e", e=NE),
                                      per_tile[:, :, :].rearrange("p e t -> p t e"), ALU.add))
            for c in range(2):
                step.then(v.tensor_tensor(rank[:, :, :], position[:, :, :], chosen[:, c, :, :], ALU.mult))
                step.then(v.tensor_reduce(slot_f[:, :, c], rank[:, :, :], AX.X, ALU.add))
            step.then(v.tensor_scalar(slot_f[:, NT - 1, :], slot_f[:, NT - 1, :], far[:, :], None, ALU.add))
            step.then(v.tensor_copy(slot_i[:, :, :], slot_f[:, :, :]))
            v.tensor_scalar(slots_i[:, :, :], slot_f[:, :, :], float(SLOTS * P - 1), None, ALU.min)
            flat = slot_i[:, :, :].rearrange("p t c -> p (t c)")
            v.tensor_scalar(slot_lane_i[:, :], flat, P - 1, None, ALU.bitwise_and)
            step.then(v.tensor_scalar(slot_tile_i[:, :], flat, 7, None, ALU.logical_shift_right))
            v.tensor_copy(slot_lane[:, :], slot_lane_i[:, :])
            step.then(v.tensor_copy(slot_tile[:, :], slot_tile_i[:, :]))
            n2 = 2 * NT
            step.then(v.tensor_tensor(tile_hot[:, :, :], slot_tile[:, :].unsqueeze(2).to_broadcast([P, n2, SLOTS]),
                                      iota[:, 0:SLOTS].unsqueeze(1).to_broadcast([P, n2, SLOTS]), ALU.is_equal))
            step.then(v.tensor_tensor(tile_hot[:, :, :], tile_hot[:, :, :],
                                      token_id[:, :, :].rearrange("p t c -> p (t c)").unsqueeze(2).to_broadcast([P, n2, SLOTS]), ALU.mult))
            for q in range(5):
                a, b = q * n2 // 5, (q + 1) * n2 // 5
                v.tensor_tensor(lane_hot[:, a:b, :], slot_lane[:, a:b].unsqueeze(2).to_broadcast([P, b - a, P]),
                                iota[:, :].unsqueeze(1).to_broadcast([P, b - a, P]), ALU.is_equal).then_inc(lane_hot_ready, 1)
            v.wait_ge(gap_exp, 1)
            step.then(v.tensor_scalar(gap[:, :], e_gap[:, :], 1.0, None, ALU.add))
            step.then(v.reciprocal(mix[:, :, 0], gap[:, :]))
            step.then(v.tensor_tensor(mix[:, :, 1], mix[:, :, 0], e_gap[:, :], ALU.mult))
            v.wait_ge(ids_summed, 1)
            v.tensor_copy(token_idx[:, :], ps[:, 2, 0:SLOTS]).then_inc(ids_ready, 1)

            v.wait_ge(biases_loaded, 32)

            def activate(s, j):
                e = v.value_load(expert_row[0:1, bass.ds(s, 1)], min_val=0, max_val=NE - 1)
                v.wait_ge(h_ready, s + 3)
                step.mark(v.tensor_tensor(h_sb[:, j, :], ps[:, 2 + j, :], b1_b[:, bass.ds(e, 1), :].rearrange("p a n -> p (a n)"), ALU.add))
                step.wait()
                v.nop().then_inc(h_taken, 1)
                v.tensor_scalar(g_sb[:, j, :], h_sb[:, j, 0:F], LIMIT, None, ALU.min).then_inc(g_ready, 1)
                step.then(v.tensor_scalar(v_sb[:, j, :], h_sb[:, j, F:F2], LIMIT, -LIMIT, ALU.min, ALU.max))
                step.then(v.scalar_tensor_tensor(out=gv_sb[:, j, :], in0=v_sb[:, j, :], scalar=1.0, in1=g_sb[:, j, :],
                                                 op0=ALU.add, op1=ALU.mult))
                v.wait_ge(sig_ready, s + 1)
                v.wait_ge(act_turned, s + 1)
                v.tensor_tensor(act_sb[:, j, :], gv_sb[:, j, :], sig_sb[:, j, :], ALU.mult).then_inc(act_ready, 1)

            def take_y(s, j, r):
                e = v.value_load(expert_row[0:1, bass.ds(s, 1)], min_val=0, max_val=NE - 1)
                v.wait_ge(y_ready, s + 3)
                v.wait_ge(y_stored[j], 16 * r + 16)
                v.tensor_tensor(y_sb[:, j, :], ps[:, 5:7, :].rearrange("p b n -> p (b n)"),
                                b2_b[:, bass.ds(e, 1), :].rearrange("p a n -> p (a n)"), ALU.add).then_inc(y_taken, 1)

            activate(0, 0)
            with v.Fori(0, SLOTS // 2 - 1) as i:
                step.rounds(i, 6)
                for j in range(2):
                    activate(2 * i + j + 1, 1 - j)
                    take_y(2 * i + j, j, i)
            step.end_rounds(SLOTS // 2 - 1)
            activate(SLOTS - 1, 1)
            take_y(SLOTS - 2, 0, SLOTS // 2 - 1)
            take_y(SLOTS - 1, 1, SLOTS // 2 - 1)

            def mix_tile(t, j, r):
                v.wait_ge(x1_loaded[j], 16 * r + 16)
                v.wait_ge(first_loaded[j], 32 * r + 32)
                step.then(v.scalar_tensor_tensor(out=partial[:, :], in0=y_first[:, j, :], scalar=mix[:, bass.ds(t, 1), 0],
                                                 in1=x1_in[:, j, :], op0=ALU.mult, op1=ALU.add))
                v.wait_ge(out_stored[j], 16 * r + 16)
                v.scalar_tensor_tensor(out=out_sb[:, j, :], in0=y_second[:, j, :], scalar=mix[:, bass.ds(t, 1), 1],
                                       in1=partial[:, :], op0=ALU.mult, op1=ALU.add).then_inc(mixed, 1)
                v.wait_ge(mixed, t + 3)

            with v.Fori(0, NT // 2) as i:
                step.rounds(i, 2)
                for j in range(2):
                    mix_tile(2 * i + j, j, i)
            step.end_rounds(NT // 2)
            mix_tile(NT - 1, 0, NT // 2)

        @block.tensor
        def _(pe):
            pe.wait_ge(counted, 1)
            pe.matmul(ps[:, 5, 0:NT - 1], ones[0:RQ, :], count_part[:, :], start=True, stop=True).then_inc(counts_summed, 1)
            pe.wait_ge(att_placed, 1)
            pe.wait_ge(wt_loaded, 16)
            for k in range(KT):
                for j in range(KT):
                    last = pe.matmul(ps[:, 6, 2 * H * k:2 * H * (k + 1)], wt_sb[:, j, k * P:(k + 1) * P],
                                     att_blk[:, j, :], start=(j == 0), stop=(j == KT - 1))
            last.then_inc(w_att_summed, 1)

            def turn(t, k):
                pe.wait_ge(xln_ready, t + 1 + XS)
                pe.wait_ge(xt_evacuated, t + 1)
                for c in range(KT):
                    last = pe.transpose(ps[:, 2 * k + c // 4, (c % 4) * P:(c % 4 + 1) * P],
                                        xln[:, k, c * P:(c + 1) * P], ident[:, :])
                last.then_inc(turned, 1)

            def logits(t, j):
                pe.wait_ge(xt_evacuated, t + 3)
                for c in range(KT):
                    last = pe.matmul(ps[:, 4, bass.ds(t * 2 * H, 2 * H)], xt_out[:, j, c, :], w_att[:, c, :],
                                     start=(c == 0), stop=(c == KT - 1))
                last.then_inc(att_done, 1)

            pe.wait_ge(consts, 5)
            turn(0, 0)
            pe.wait_ge(w_att_ready, 1)
            with pe.Fori(0, HALF) as i:
                for j in range(XS):
                    turn(i * XS + j + 1, (j + 1) % 2)
                    logits(i * XS + j, j)
            logits(NT - 1, 0)

            def project(t, j, r):
                pe.wait_ge(xt_loaded[j], 16 * r + 16)
                pe.wait_ge(xp_evacuated, t + 1)
                for c in range(KT):
                    for n in range(2):
                        last = pe.matmul(ps[:, 2 * j + n, :], xt_in[:, j, c, :], w_sb[:, c, n * 512:(n + 1) * 512],
                                         start=(c == 0), stop=(c == KT - 1))
                last.then_inc(projected, 1)

            def fetch(c, j):
                pe.wait_ge(hot_ready, c + 1)
                pe.wait_ge(dst_taken, c + 1)
                for g in range(4):
                    pe.wait_ge(src_taken, 4 * c + g + 1)
                    for q in range(4):
                        e = (4 * g + q) * P
                        for n in range(3):
                            last = pe.matmul(ps[:, 4 + g % 2, q * NT * H:(q + 1) * NT * H], lows_hot[:, j, 0, e:e + P],
                                             node_parts[:, n, :, 0:H], start=(n == 0), stop=(n == 2))
                    last.then_inc(src_fetched, 1)
                    for q in range(4):
                        m = 4 * g + q
                        t = pe.value_load(tile_row[0:1, bass.ds(c * CH + m, 1)], min_val=0, max_val=NT - 1)
                        for n in range(3):
                            last = pe.matmul(ps[:, 6 + j, m * 2 * H:(m + 1) * 2 * H],
                                             lows_hot[:, j, 1, m * P:(m + 1) * P],
                                             node_parts[:, n, bass.ds(t, 1), :].rearrange("p a m -> p (a m)"),
                                             start=(n == 0), stop=(n == 2))
                last.then_inc(dst_fetched, 1)

            pe.wait_ge(w_loaded, 16)
            project(0, 0, 0)
            project(1, 1, 0)
            pe.wait_ge(rows_ready, 1)
            pe.wait_ge(parts_ready, 1)
            for n, rows in enumerate((hi_rows, src_rows, rel_rows)):
                for b in range(4):
                    last = pe.transpose(ps[:, 4 + n, b * PQ:(b + 1) * PQ], rows[:, b * P:(b + 1) * P], ident[0:PQ, 0:PQ])
            last.then_inc(rows_turned, 1)
            pe.wait_ge(cols_taken, 1)
            pe.wait_ge(tile_row_loaded, 16)
            with pe.Fori(0, STEPS2) as i:
                for j in range(2):
                    project(2 * i + j + 2, j, i + 1)
                    fetch(4 * i + 2 * j, 0)
                    fetch(4 * i + 2 * j + 1, 1)
            t = 2 * STEPS2 + 2
            project(t, 0, t // 2)
            fetch(NCH - 2, 0)
            fetch(NCH - 1, 1)
            t += 1
            project(t, 1, t // 2)
            pe.wait_ge(as_ready, 1)
            pe.wait_ge(dst_taken, NCH + 2)
            for h in range(H):
                for b in range(4):
                    last = pe.transpose(ps[0:PQ, 4 + h, b * P:(b + 1) * P],
                                        as_col[:, :, h].rearrange("p (q b) -> p b q", b=4)[:, b, :], ident[:, :])
            last.then_inc(as_turned, 1)
            t0 = t + 1
            for t in range(t0, t0 + 2):
                project(t, t % 2, t // 2)
            pe.wait_ge(ends_ready, 1)
            pe.wait_ge(as_rows_ready, 1)
            for n in range(4):
                last = pe.transpose(ps[0:H, 4, n * PQ:(n + 1) * PQ], ends[:, n, :], ident[0:PQ, 0:PQ])
            last.then_inc(ends_turned, 1)
            t += 1
            project(t, t % 2, t // 2)
            pe.wait_ge(carry_ready, 1)
            for n in range(3):
                last = pe.transpose(ps[0:PQ, 5, n * H:(n + 1) * H], carry_t[:, n, :], ident[0:H, 0:H])
            last.then_inc(carry_turned, 1)
            t += 1
            project(t, t % 2, t // 2)
            pe.wait_ge(max_ready, 1)
            for h in range(H):
                for b in range(4):
                    last = pe.transpose(ps[:, 4 + h, b * PQ:(b + 1) * PQ], as_rows[:, h, b * P:(b + 1) * P], ident[0:PQ, 0:PQ])
            last.then_inc(max_turned, 1)
            pe.wait_ge(max_taken, H)
            for b in range(4):
                last = pe.transpose(ps[:, 4, b * PQ:(b + 1) * PQ], last_rows[:, b * P:(b + 1) * P], ident[0:PQ, 0:PQ])
            last.then_inc(max_turned, 1)
            for t in range(t + 1, NT):
                project(t, t % 2, t // 2)

            pe.wait_ge(weights_ready, 1)
            with pe.Fori(0, NCH // 2) as i:
                for g in range(2):
                    c = 2 * i + g
                    pe.wait_ge(hot_built, c + 1)
                    _, tiles = nc.values_load_multi_w_load_instructions(
                        tile_row[0:1, bass.ds(c * CH, CH)], engines=[mybir.EngineType.PE], min_val=0, max_val=NT - 1)
                    for j in range(CH):
                        half = tiles[j] % 2
                        pe.wait_ge(acc_free, tiles[j] + 1)
                        pe.wait_ge(weighted_ready, c * CH + j + 1)
                        pe.wait_ge(message_loaded[j % GR], 16 * (c * (CH // GR) + j // GR + 1))
                        for h in range(H):
                            pe.matmul(ps[:, bass.ds(half * 2 + h // 2, 1), (h % 2) * C:(h % 2 + 1) * C].rearrange("p a n -> p (a n)"),
                                      weighted[:, j % GR, h, :], messages[:, j % GR, h * C:(h + 1) * C],
                                      start=False, stop=True, skip_group_check=True)
                        pe.matmul(ps[:, bass.ds(half + 4, 1), 0:NCOL].rearrange("p a n -> p (a n)"),
                                  dst_hot[:, g * CH + j, :], pair_cols[:, bass.ds(c * CH + j, 1), :].rearrange("p a n -> p (a n)"),
                                  start=False, stop=True, skip_group_check=True).then_inc(pair_done, 1)

            pe.wait_ge(selected_ready, 1)
            chosen_flat = selected[:, :, :].rearrange("p t e -> p (t e)")
            pe.matmul(ps[:, 0, 0:NT * NE], upper[:, :], chosen_flat, start=True, stop=True)
            pe.matmul(ps[:, 1, 0:NT * NE], ones[:, :], chosen_flat, start=True, stop=True).then_inc(ranks_summed, 1)
            for q in range(5):
                pe.wait_ge(lane_hot_ready, q + 1)
                for n in range(q * 2 * NT // 5, (q + 1) * 2 * NT // 5):
                    last = pe.matmul(ps[:, 2, 0:SLOTS], lane_hot[:, n, :], tile_hot[:, n, :],
                                     start=(n == 0), stop=(n == 2 * NT - 1))
            last.then_inc(ids_summed, 1)
            pe.wait_ge(ids_ready, 1)

            def turn_tokens(s, j, r):
                pe.wait_ge(tokens_loaded[j], 16 * r + 16)
                pe.wait_ge(tokens_ready, s + 2)
                for c in range(KT):
                    last = pe.transpose(ps[:, c // 4, (c % 4) * P:(c % 4 + 1) * P], tokens_in[:, j, c * P:(c + 1) * P], ident[:, :])
                last.then_inc(tokens_turned, 1)

            def rise(s, j):
                e = pe.value_load(expert_row[0:1, bass.ds(s, 1)], min_val=0, max_val=NE - 1)
                pe.wait_ge(expert_seen, e + 1)
                pe.wait_ge(tokens_ready, s + 3)
                pe.wait_ge(h_taken, s + 1)
                for c in range(KT):
                    last = pe.matmul(ps[:, 2 + j, :], tokens_t[:, j, c, :],
                                     w1_sb[:, bass.ds(e % 2, 1), c, :].rearrange("p a n -> p (a n)"),
                                     start=(c == 0), stop=(c == KT - 1))
                last.then_inc(h_ready, 1)

            def turn_act(s, j):
                pe.wait_ge(act_ready, s + 1)
                pe.wait_ge(act_t_ready, s + 2)
                for c in range(FT):
                    last = pe.transpose(ps[:, 4, c * P:(c + 1) * P], act_sb[:, j, c * P:(c + 1) * P], ident[:, :])
                last.then_inc(act_turned, 1)

            def fall(s, j):
                e = pe.value_load(expert_row[0:1, bass.ds(s, 1)], min_val=0, max_val=NE - 1)
                pe.wait_ge(act_t_ready, s + 3)
                pe.wait_ge(y_taken, s + 1)
                for n in range(2):
                    for c in range(FT):
                        last = pe.matmul(ps[:, 5 + n, :], act_t[:, j, c, :],
                                         w2_sb[:, bass.ds(e % 2, 1), c, n * 512:(n + 1) * 512].rearrange("p a n -> p (a n)"),
                                         start=(c == 0), stop=(c == FT - 1))
                last.then_inc(y_ready, 1)

            turn_tokens(0, 0, 0)
            turn_tokens(1, 1, 0)
            rise(0, 0)
            with pe.Fori(0, SLOTS // 4 - 1) as i:
                for j in range(4):
                    s = 4 * i + j + 1
                    rise(s, (j + 1) % 2)
                    turn_act(s - 1, j % 2)
                    turn_tokens(s + 1, (j + 2) % 4, i + (j + 2) // 4)
                    fall(s - 1, j % 2)
            for s in range(SLOTS - 3, SLOTS):
                rise(s, s % 2)
                turn_act(s - 1, (s - 1) % 2)
                if s + 1 < SLOTS:
                    turn_tokens(s + 1, (s + 1) % 4, (s + 1) // 4)
                fall(s - 1, (s - 1) % 2)
            turn_act(SLOTS - 1, 1)
            fall(SLOTS - 1, 1)


def kernel(**inputs):
    import concourse.bacc as _bacc
    import numpy as _np
    from concourse import mybir as _mybir
    from concourse.bass_utils import run_bass_kernel_spmd as _run

    a = {name: _np.asarray(value) for name, value in inputs.items()}
    w, w1, b1, w2 = a["L0_gnn_W"], a["L0_ffn_dense_1_w"], a["L0_ffn_dense_1_b"], a["L0_ffn_dense_2_w"]
    experts, f2, d = w1.shape
    p = 128
    laid_out = {
        "x": a["x"],
        "src": a["src"],
        "dst": a["dst"],
        "w": w,
        "w_t": w.T.reshape(-1, p, w.shape[0]).transpose(1, 0, 2),
        "att_src": a["L0_gnn_att_src"],
        "att_dst": a["L0_gnn_att_dst"],
        "bias": a["L0_gnn_bias"],
        "gate_t": a["L0_ffn_gate_w"].T,
        "w1": _np.concatenate([w1[:, 0::2], w1[:, 1::2]], 1).transpose(0, 2, 1)
              .reshape(experts, d // p, p, f2).transpose(0, 2, 1, 3),
        "b1": _np.concatenate([b1[:, 0::2], b1[:, 1::2]], 1),
        "w2": w2.transpose(0, 2, 1).reshape(experts, f2 // 2 // p, p, d).transpose(0, 2, 1, 3),
        "b2": a["L0_ffn_dense_2_b"],
    }
    nc = _bacc.Bacc("TRN2", target_bir_lowering=False, num_devices=1)
    arrays, args = {}, {}
    for name, value in laid_out.items():
        value = _np.ascontiguousarray(value)
        arrays[f"in_{name}"] = value
        args[name] = nc.dram_tensor(f"in_{name}", value.shape, _mybir.dt.from_np(value.dtype), kind="ExternalInput").ap()
    out = nc.dram_tensor("out_0", a["x"].shape, _mybir.dt.float32, kind="ExternalOutput").ap()
    gat_moe_kernel(nc, **args, out=out)
    result = _run(nc, [arrays], core_ids=[0])
    return result.results[0]["out_0"]
```
